# Optimizing a Trainium2 kernel written in Bass

```python
import numpy as np
import jax
import jax.numpy as jnp

def _softmax(x, axis=-1):
    return jax.nn.softmax(x, axis=axis)

def _gelu(x):
    return jax.nn.gelu(x, approximate=True)

def _silu(x):
    return jax.nn.silu(x)

def _sigmoid(x):
    return jax.nn.sigmoid(x)

def _layernorm(x, axis=-1, eps=1e-05):
    m = jnp.mean(x, axis=axis, keepdims=True)
    v = jnp.var(x, axis=axis, keepdims=True)
    return (x - m) / jnp.sqrt(v + eps)

def _scatter_add(tgt, idx, src, axis=0):
    return tgt.at[idx].add(src)

def _segment_sum(src, seg, n):
    return jax.ops.segment_sum(src, seg, n)
kernel_name = 'mk_dlrm_tower_d1_rec_r8_9c1a83'

def setup_inputs(seed: int=0):
    np.random.seed(seed)
    _w = jnp.asarray

    def _rec_inputs():
        import jax
        import jax.numpy as jnp
        _tk = jax.random.key(seed)
        ids = jnp.stack([jax.random.randint(jax.random.fold_in(_tk, 200 + f), (512,), 0, v, jnp.int32) for f, v in enumerate([125000, 12500, 1250, 1250, 1250, 1000, 1250, 12500, 12500, 1000, 1250, 1250, 1250, 1250, 1250, 12500, 1250, 1250, 1250, 12500, 1250, 1000, 1000, 12500, 1250, 12500])], axis=1)
        tbl_0 = 0.05 * jax.random.normal(jax.random.fold_in(_tk, 500 + 0), (125000, 128), jnp.float32)
        tbl_1 = 0.05 * jax.random.normal(jax.random.fold_in(_tk, 500 + 1), (12500, 128), jnp.float32)
        tbl_2 = 0.05 * jax.random.normal(jax.random.fold_in(_tk, 500 + 2), (1250, 128), jnp.float32)
        tbl_3 = 0.05 * jax.random.normal(jax.random.fold_in(_tk, 500 + 3), (1250, 128), jnp.float32)
        tbl_4 = 0.05 * jax.random.normal(jax.random.fold_in(_tk, 500 + 4), (1250, 128), jnp.float32)
        tbl_5 = 0.05 * jax.random.normal(jax.random.fold_in(_tk, 500 + 5), (1000, 128), jnp.float32)
        tbl_6 = 0.05 * jax.random.normal(jax.random.fold_in(_tk, 500 + 6), (1250, 128), jnp.float32)
        tbl_7 = 0.05 * jax.random.normal(jax.random.fold_in(_tk, 500 + 7), (12500, 128), jnp.float32)
        tbl_8 = 0.05 * jax.random.normal(jax.random.fold_in(_tk, 500 + 8), (12500, 128), jnp.float32)
        tbl_9 = 0.05 * jax.random.normal(jax.random.fold_in(_tk, 500 + 9), (1000, 128), jnp.float32)
        tbl_10 = 0.05 * jax.random.normal(jax.random.fold_in(_tk, 500 + 10), (1250, 128), jnp.float32)
        tbl_11 = 0.05 * jax.random.normal(jax.random.fold_in(_tk, 500 + 11), (1250, 128), jnp.float32)
        tbl_12 = 0.05 * jax.random.normal(jax.random.fold_in(_tk, 500 + 12), (1250, 128), jnp.float32)
        tbl_13 = 0.05 * jax.random.normal(jax.random.fold_in(_tk, 500 + 13), (1250, 128), jnp.float32)
        tbl_14 = 0.05 * jax.random.normal(jax.random.fold_in(_tk, 500 + 14), (1250, 128), jnp.float32)
        tbl_15 = 0.05 * jax.random.normal(jax.random.fold_in(_tk, 500 + 15), (12500, 128), jnp.float32)
        tbl_16 = 0.05 * jax.random.normal(jax.random.fold_in(_tk, 500 + 16), (1250, 128), jnp.float32)
        tbl_17 = 0.05 * jax.random.normal(jax.random.fold_in(_tk, 500 + 17), (1250, 128), jnp.float32)
        tbl_18 = 0.05 * jax.random.normal(jax.random.fold_in(_tk, 500 + 18), (1250, 128), jnp.float32)
        tbl_19 = 0.05 * jax.random.normal(jax.random.fold_in(_tk, 500 + 19), (12500, 128), jnp.float32)
        tbl_20 = 0.05 * jax.random.normal(jax.random.fold_in(_tk, 500 + 20), (1250, 128), jnp.float32)
        tbl_21 = 0.05 * jax.random.normal(jax.random.fold_in(_tk, 500 + 21), (1000, 128), jnp.float32)
        tbl_22 = 0.05 * jax.random.normal(jax.random.fold_in(_tk, 500 + 22), (1000, 128), jnp.float32)
        tbl_23 = 0.05 * jax.random.normal(jax.random.fold_in(_tk, 500 + 23), (12500, 128), jnp.float32)
        tbl_24 = 0.05 * jax.random.normal(jax.random.fold_in(_tk, 500 + 24), (1250, 128), jnp.float32)
        tbl_25 = 0.05 * jax.random.normal(jax.random.fold_in(_tk, 500 + 25), (12500, 128), jnp.float32)
        _rk = jax.random.fold_in(_tk, 7)
        r_dense_features = -0.000292821 + 1.00034 * jax.random.normal(jax.random.fold_in(_rk, 101), (512, 128), jnp.float32)
        W_top1 = 0.0405887 * jax.random.normal(jax.random.fold_in(_tk, 801), (607, 512), jnp.float32)
        W_top2 = 0.0441942 * jax.random.normal(jax.random.fold_in(_tk, 802), (512, 256), jnp.float32)
        W_top3 = 0.0625 * jax.random.normal(jax.random.fold_in(_tk, 803), (256, 1), jnp.float32)
        b_top1 = jnp.zeros((512,), jnp.float32)
        b_top2 = jnp.zeros((256,), jnp.float32)
        return (r_dense_features, ids, tbl_0, tbl_1, tbl_2, tbl_3, tbl_4, tbl_5, tbl_6, tbl_7, tbl_8, tbl_9, tbl_10, tbl_11, tbl_12, tbl_13, tbl_14, tbl_15, tbl_16, tbl_17, tbl_18, tbl_19, tbl_20, tbl_21, tbl_22, tbl_23, tbl_24, tbl_25, W_top1, b_top1, W_top2, b_top2, W_top3)
    r_dense_features, ids, tbl_0, tbl_1, tbl_2, tbl_3, tbl_4, tbl_5, tbl_6, tbl_7, tbl_8, tbl_9, tbl_10, tbl_11, tbl_12, tbl_13, tbl_14, tbl_15, tbl_16, tbl_17, tbl_18, tbl_19, tbl_20, tbl_21, tbl_22, tbl_23, tbl_24, tbl_25, W_top1, b_top1, W_top2, b_top2, W_top3 = _rec_inputs()

    def _L0_rec_setup():
        import jax, jax.numpy as jnp
        import numpy as np
        F = 26
        _TRIU_I, _TRIU_J = np.triu_indices(F + 1, k=1)
        key = jax.random.key(seed)
        k1, k2 = jax.random.split(key)
        B, D = (4096, 128)
        dense_features = jax.random.normal(k1, (B, D), dtype=jnp.float32)
        sparse_features = jax.random.normal(k2, (B, F, D), dtype=jnp.float32)
        return {'dense_features': dense_features, 'sparse_features': sparse_features}
    _L0_rec_all = _L0_rec_setup()
    _L0_rec_in = {k: v for k, v in _L0_rec_all.items() if k in ()}
    del _L0_rec_all
    return {'r_dense_features': r_dense_features, 'ids': ids, 'tbl_0': tbl_0, 'tbl_1': tbl_1, 'tbl_2': tbl_2, 'tbl_3': tbl_3, 'tbl_4': tbl_4, 'tbl_5': tbl_5, 'tbl_6': tbl_6, 'tbl_7': tbl_7, 'tbl_8': tbl_8, 'tbl_9': tbl_9, 'tbl_10': tbl_10, 'tbl_11': tbl_11, 'tbl_12': tbl_12, 'tbl_13': tbl_13, 'tbl_14': tbl_14, 'tbl_15': tbl_15, 'tbl_16': tbl_16, 'tbl_17': tbl_17, 'tbl_18': tbl_18, 'tbl_19': tbl_19, 'tbl_20': tbl_20, 'tbl_21': tbl_21, 'tbl_22': tbl_22, 'tbl_23': tbl_23, 'tbl_24': tbl_24, 'tbl_25': tbl_25, 'W_top1': W_top1, 'b_top1': b_top1, 'W_top2': W_top2, 'b_top2': b_top2, 'W_top3': W_top3}

def reference(r_dense_features, ids, tbl_0, tbl_1, tbl_2, tbl_3, tbl_4, tbl_5, tbl_6, tbl_7, tbl_8, tbl_9, tbl_10, tbl_11, tbl_12, tbl_13, tbl_14, tbl_15, tbl_16, tbl_17, tbl_18, tbl_19, tbl_20, tbl_21, tbl_22, tbl_23, tbl_24, tbl_25, W_top1, b_top1, W_top2, b_top2, W_top3):
    import jax
    import jax.numpy as jnp

    def _L0_rec_ref(dense_features, sparse_features):
        import jax, jax.numpy as jnp
        import numpy as np
        F = 26
        _TRIU_I, _TRIU_J = np.triu_indices(F + 1, k=1)
        combined = jnp.concatenate([dense_features[:, None, :], sparse_features], axis=1)
        interactions = jnp.einsum('bfd,bgd->bfg', combined, combined)
        interactions_flat = interactions[:, _TRIU_I, _TRIU_J]
        return jnp.concatenate([dense_features, interactions_flat], axis=1)
    e = jnp.stack([tbl_0[ids[:, 0]], tbl_1[ids[:, 1]], tbl_2[ids[:, 2]], tbl_3[ids[:, 3]], tbl_4[ids[:, 4]], tbl_5[ids[:, 5]], tbl_6[ids[:, 6]], tbl_7[ids[:, 7]], tbl_8[ids[:, 8]], tbl_9[ids[:, 9]], tbl_10[ids[:, 10]], tbl_11[ids[:, 11]], tbl_12[ids[:, 12]], tbl_13[ids[:, 13]], tbl_14[ids[:, 14]], tbl_15[ids[:, 15]], tbl_16[ids[:, 16]], tbl_17[ids[:, 17]], tbl_18[ids[:, 18]], tbl_19[ids[:, 19]], tbl_20[ids[:, 20]], tbl_21[ids[:, 21]], tbl_22[ids[:, 22]], tbl_23[ids[:, 23]], tbl_24[ids[:, 24]], tbl_25[ids[:, 25]]], axis=1)
    z = _L0_rec_ref(r_dense_features, e)
    z = z.reshape(z.shape[0], -1)
    h = jnp.concatenate([z, r_dense_features], axis=1)
    h = jnp.maximum(h @ W_top1 + b_top1, 0.0)
    h = jnp.maximum(h @ W_top2 + b_top2, 0.0)
    y = h @ W_top3
    return y

_drawn_inputs = setup_inputs


def setup_inputs(seed=0):
    import zlib

    import numpy as np

    out = dict(_drawn_inputs(seed))
    spreads = {'b_top1': (0.0, 0.1), 'b_top2': (0.0, 0.1)}
    factors = {}
    for name, (base, spread) in spreads.items():
        noise = np.random.default_rng([zlib.crc32(name.encode()), seed]).standard_normal(out[name].shape)
        drawn = base * np.exp(spread * noise) if base else spread * noise
        out[name] = jnp.asarray(drawn.astype(out[name].dtype))
    for name, factor in factors.items():
        out[name] = (out[name] * factor).astype(out[name].dtype)
    return out
```

```python
import concourse.bass as bass
from concourse import mybir
from contextlib import ExitStack

B = 512
D = 128
N_TABLES = 26
F = N_TABLES + 1
P = 128
TILES = B // P
SLOTS = 32
COLS = 28
PAIR_COLS = (F + 1) // 2
CHUNKS = (PAIR_COLS + 3) // 4
H1, H2 = 512, 256
PART = 125
ONEHOT = [5, 9, 21, 22, 2, 3, 4]
GATHERED = [f for f in range(N_TABLES) if f not in ONEHOT]
FEATURE_OF_SLOT = [0] + [f + 1 for f in ONEHOT] + [f + 1 for f in GATHERED]
SLOT_ONEHOT = 1
SLOT_GATHERED = 1 + len(ONEHOT)
GROUP = 4
GROUPS = [list(range(g, min(g + GROUP, len(GATHERED)))) for g in range(0, len(GATHERED), GROUP)]
HALF = 64
BIAS_ROW = 64


def tower(nc, dense, ids, ids_by_table, tables, w1_pairs, w1_dense, b1, w2, b2, w3, identity, row_ids,
          pair_mask, out):
    fp32, f32r, i32 = mybir.dt.float32, mybir.dt.float32r, mybir.dt.int32
    ALU, ACT = mybir.AluOpType, mybir.ActivationFunctionType
    n_onehot = len(ONEHOT)
    rows_per_part = [tables[f].shape[0] // PART for f in ONEHOT]
    max_rows = max(rows_per_part)

    with ExitStack() as ctx:
        def sb(name, shape, dt=fp32):
            return ctx.enter_context(nc.sbuf_tensor(name, shape, dt))

        def sem(name):
            return ctx.enter_context(nc.semaphore(name))

        index = sb("index", [P, TILES, N_TABLES], i32)
        onehot_ids = sb("onehot_ids", [P, n_onehot, B], i32)
        ident = sb("ident", [P, P])
        row_id = sb("row_id", [P, 2, max_rows])
        mask = sb("mask", [P, CHUNKS], i32)
        dense_rows = sb("dense_rows", [P, TILES, D])
        rows = sb("rows", [P, TILES, len(GATHERED), D])
        XT = sb("XT", [P, TILES, P, SLOTS])
        denseT = sb("denseT", [P, TILES, P])
        table = [sb(f"table{i}", [P, max_rows, D]) for i in range(2)]
        table_hi = [sb(f"table_hi{i}", [P, max_rows, D], f32r) for i in range(2)]
        table_lo = [sb(f"table_lo{i}", [P, max_rows, D], f32r) for i in range(2)]
        RING = 6
        onehot = [sb(f"onehot{i}", [P, B], f32r) for i in range(RING)]
        Z = sb("Z", [P, CHUNKS, TILES, P])
        w1p = sb("w1p", [P, CHUNKS, H1])
        w1d = sb("w1d", [P, 2, H1])
        w1s = sb("w1s", [P, H1])
        w2s = sb("w2s", [P, H1 // P, H2])
        w3s = sb("w3s", [P, H2 // P])
        b2s = sb("b2s", [P, H2 // P])
        h1 = sb("h1", [P, 2, H1 // P, P])
        h2 = sb("h2", [P, 2, H2 // P, P])
        y = sb("y", [1, P, TILES])

        gram = ctx.enter_context(nc.psum_tensor("gram", [P, 4, 512], fp32))
        featT = ctx.enter_context(nc.psum_tensor("featT", [P, 2, 512], fp32))
        ps1 = ctx.enter_context(nc.psum_tensor("ps1", [P, H1 // P, P], fp32))
        ps2 = ctx.enter_context(nc.psum_tensor("ps2", [P, 512], fp32))
        ps3 = ps2[0:1, 2 * P:3 * P]

        index_loaded = sem("index_loaded")
        consts_loaded = sem("consts_loaded")
        mask_loaded = sem("mask_loaded")
        ids_loaded = sem("ids_loaded")
        dense_loaded = sem("dense_loaded")
        w1_loaded = sem("w1_loaded")
        w2_loaded = sem("w2_loaded")
        table_loaded = [sem(f"table_loaded{i}") for i in range(2)]
        gathered = [[sem(f"gathered{t}_{g}") for g in range(len(GROUPS))] for t in range(TILES)]
        padded = sem("padded")
        w1_summed = sem("w1_summed")
        hi_ready = sem("hi_ready")
        lo_ready = sem("lo_ready")
        onehot_ready = sem("onehot_ready")
        onehot_used = sem("onehot_used")
        featT_ready = sem("featT_ready")
        featT_act = sem("featT_act")
        featT_dve = sem("featT_dve")
        gram_ready = sem("gram_ready")
        base_copied = sem("base_copied")
        pairs_done = sem("pairs_done")
        ps1_ready = sem("ps1_ready")
        h1_ready = sem("h1_ready")
        ps2_ready = sem("ps2_ready")
        h2_ready = sem("h2_ready")
        ps3_ready = sem("ps3_ready")
        y_ready = sem("y_ready")
        stored = sem("stored")

        banks = [("dense", 0, 0)]
        banks += [("onehot", i, 0) for i in range(n_onehot)]
        banks += [("rows", t, g) for t in range(TILES) for g in range(len(GROUPS))]
        on_act = [kind == "onehot" or n % 2 == 0 for n, (kind, _, _) in enumerate(banks)]

        def written(n):
            if banks[n][0] == "onehot":
                return onehot_used, sum(rows_per_part[:banks[n][1] + 1])
            return featT_ready, sum(kind != "onehot" for kind, _, _ in banks[:n + 1])

        def copied_out(n):
            s = featT_act if on_act[n] else featT_dve
            return s, sum(on_act[m] == on_act[n] for m in range(n + 1))

        def copy_bank(n, copy):
            kind, a, g = banks[n]
            src = featT[:, n % 2, :]
            if kind == "dense":
                src = src.rearrange("d (t p) -> d t p", t=TILES)
                copy(denseT[:, :, :], src)
                return copy(XT[:, :, :, 0], src)
            if kind == "onehot":
                return copy(XT[:, :, :, SLOT_ONEHOT + a], src.rearrange("d (p t) -> d t p", t=TILES))
            k = len(GROUPS[g])
            s = SLOT_GATHERED + GROUPS[g][0]
            return copy(XT[:, a, :, s:s + k].rearrange("d p s -> d s p"),
                        src[:, 0:k * P].rearrange("d (s p) -> d s p", s=k))

        def pair_block(batch, i, j, first, count):
            t, half = divmod(batch, 2)
            src = gram[32 * i:32 * i + 32, :, 0:4 * 4 * COLS].rearrange("p b (q c) -> p b q c", q=4)
            at = COLS * i + first
            src = src[:, :, :, at:at + 4 * (count - 1) + 1:4]
            dst = Z[32 * j:32 * j + 32, 0:count, t, HALF * half:HALF * half + HALF]
            dst = dst.rearrange("p k (b q i) -> p b q k i", b=4, q=4)[:, :, :, :, i]
            return dst, src

        block = ctx.enter_context(nc.Block())

        @block.sync
        def _(sp):
            sp.dma_start(index[:, :, :], ids.rearrange("(p t) f -> p t f", t=TILES)).then_inc(index_loaded, 16)
            sp.dma_start(row_id[:, :, :], row_ids).then_inc(consts_loaded, 16)

            def load_table(i):
                r = rows_per_part[i]
                if i >= 2:
                    sp.wait_ge(hi_ready, i - 1)
                    sp.wait_ge(lo_ready, i - 1)
                sp.dma_start(table[i % 2][0:PART, 0:r, :],
                             tables[ONEHOT[i]].rearrange("(p r) d -> p r d", r=r)).then_inc(table_loaded[i % 2], 16)

            sp.dma_start(onehot_ids[0:PART, :, :],
                         ids_by_table.unsqueeze(0).to_broadcast([PART, n_onehot, B])).then_inc(ids_loaded, 16)
            load_table(0)
            sp.dma_start(ident[:, :], identity).then_inc(consts_loaded, 16)
            sp.dma_start(dense_rows[:, :, :], dense.rearrange("(p t) d -> p t d", t=TILES)).then_inc(dense_loaded, 16)
            load_table(1)
            sp.dma_start(w1d[:, :, :], w1_dense.rearrange("(c p) n -> p c n", c=2)).then_inc(w1_loaded, 16)
            sp.dma_start(mask[:, :], pair_mask).then_inc(mask_loaded, 16)
            for i in range(2, n_onehot):
                load_table(i)
            sp.dma_start(w1p[:, 0:CHUNKS - 1, :], w1_pairs[:, 0:CHUNKS - 1, :]).then_inc(w1_loaded, 16)
            sp.dma_start(w1p[0:BIAS_ROW, CHUNKS - 1, :], w1_pairs[0:BIAS_ROW, CHUNKS - 1, :]).then_inc(w1_loaded, 16)
            sp.dma_start(w1p[BIAS_ROW:BIAS_ROW + 1, CHUNKS - 1, :], b1.unsqueeze(0)).then_inc(w1_loaded, 16)
            sp.dma_start(w2s[:, :, :], w2.rearrange("(c p) n -> p c n", p=P)).then_inc(w2_loaded, 16)
            for c in range(H2 // P):
                sp.dma_start(w3s[:, c:c + 1], w3[c * P:(c + 1) * P, :]).then_inc(w2_loaded, 16)
                sp.dma_start(b2s[:, c:c + 1], b2[c * P:(c + 1) * P].unsqueeze(1)).then_inc(w2_loaded, 16)
            sp.wait_ge(y_ready, TILES)
            sp.dma_start(out.rearrange("(o p t) n -> o p (t n)", o=1, t=TILES), y[:, :, :]).then_inc(stored, 16)
            sp.wait_ge(stored, 16)

        @block.gpsimd
        def _(pool):
            pool.wait_ge(index_loaded, 16)
            for t in range(TILES):
                for g, group in enumerate(GROUPS):
                    for k in group:
                        f = GATHERED[k]
                        pool.indirect_dma_start(
                            rows[:, t, k, :], None, tables[f],
                            bass.IndirectOffsetOnAxis(ap=index[:, t, f:f + 1], axis=0),
                        ).then_inc(gathered[t][g], 16)

        @block.scalar
        def _(act):
            def copy(dst, src):
                return nc.scalar.activation(dst, src, ACT.Copy)

            def copy_out(n):
                if on_act[n]:
                    act.wait_ge(*written(n))
                    copy_bank(n, copy).then_inc(featT_act, 1)

            copy_out(0)
            for i in range(n_onehot):
                r = rows_per_part[i]
                act.wait_ge(table_loaded[i % 2], 16 * (i // 2 + 1))
                if i >= 2:
                    act.wait_ge(*written(1 + i - 2))
                copy(table_hi[i % 2][0:PART, 0:r, :], table[i % 2][0:PART, 0:r, :]).then_inc(hi_ready, 1)
                if i >= 1:
                    copy_out(i)
            copy_out(n_onehot)
            n = n_onehot + 1
            for t in range(TILES):
                for g in range(len(GROUPS)):
                    copy_out(n)
                    n += 1
                for half in range(2):
                    batch = 2 * t + half
                    act.wait_ge(gram_ready, batch + 1)
                    if batch == 0:
                        act.wait_ge(padded, 2)
                    for i in range(4):
                        for j in range(4):
                            count = len(range(j, PAIR_COLS, 4))
                            dst, src = pair_block(batch, i, j, PAIR_COLS - 1 + j, count)
                            copy(dst, src).then_inc(base_copied, 1)
                if t == 0:
                    act.wait_ge(w2_loaded, 16 * 5)
                act.wait_ge(ps1_ready, t + 1)
                if t >= 2:
                    act.wait_ge(ps2_ready, t - 1)
                nc.scalar.activation(h1[:, t % 2, :, :], ps1[:, :, :], ACT.Relu).then_inc(h1_ready, 1)
                act.wait_ge(ps2_ready, t + 1)
                if t >= 2:
                    act.wait_ge(ps3_ready, t - 1)
                for c in range(H2 // P):
                    nc.scalar.activation(h2[:, t % 2, c, :], ps2[:, c * P:(c + 1) * P], ACT.Relu,
                                         bias=b2s[:, c:c + 1]).then_inc(h2_ready, 1)
                act.wait_ge(ps3_ready, t + 1)
                copy(y[:, :, t], ps3).then_inc(y_ready, 1)

        @block.vector
        def _(dve):
            def copy(dst, src):
                return nc.vector.tensor_copy(dst, src)

            def copy_out(n):
                if not on_act[n]:
                    dve.wait_ge(*written(n))
                    copy_bank(n, copy).then_inc(featT_dve, 1)

            nc.vector.memset(XT[:, :, :, F:SLOTS], 0.0).then_inc(padded, 1)
            nc.vector.memset(Z[BIAS_ROW:BIAS_ROW + 32, CHUNKS - 1, :, :], 1.0).then_inc(padded, 1)
            n = 0
            dve.wait_ge(consts_loaded, 32)
            dve.wait_ge(ids_loaded, 16)
            blocks = 0
            for i in range(n_onehot):
                r = rows_per_part[i]
                for c in range(r):
                    if blocks >= RING:
                        dve.wait_ge(onehot_used, blocks - RING + 1)
                    which = 0 if r == min(rows_per_part) else 1
                    nc.vector.tensor_scalar(onehot[blocks % RING][0:PART, :], onehot_ids[0:PART, i, :],
                                            row_id[0:PART, which, c:c + 1], None,
                                            ALU.is_equal).then_inc(onehot_ready, 1)
                    blocks += 1
                    if c == 0:
                        dve.wait_ge(hi_ready, i + 1)
                        if i >= 2:
                            dve.wait_ge(*written(1 + i - 2))
                        nc.vector.tensor_tensor(table_lo[i % 2][0:PART, 0:r, :], table[i % 2][0:PART, 0:r, :],
                                                table_hi[i % 2][0:PART, 0:r, :].bitcast(fp32),
                                                ALU.subtract).then_inc(lo_ready, 1)
            dve.wait_ge(w1_loaded, 16 * 4)
            nc.vector.tensor_tensor(w1s[:, :], w1d[:, 0, :], w1d[:, 1, :], ALU.add).then_inc(w1_summed, 1)
            dve.wait_ge(mask_loaded, 16)
            n = n_onehot + 1
            for t in range(TILES):
                for g in range(len(GROUPS)):
                    copy_out(n)
                    n += 1
                for half in range(2):
                    batch = 2 * t + half
                    for i in range(4):
                        dve.wait_ge(base_copied, 16 * batch + 4 * (i + 1))
                        for j in range(4):
                            count = len(range(j, PAIR_COLS - 1, 4))
                            dst, src = pair_block(batch, i, j, j, count)
                            m = mask[32 * j:32 * j + 32, 0:count].unsqueeze(1).unsqueeze(1)
                            nc.vector.copy_predicated(dst, m.to_broadcast([32, 4, 4, count]),
                                                      src).then_inc(pairs_done, 1)

        @block.tensor
        def _(pe):
            def bank_free(n):
                if n >= 2:
                    pe.wait_ge(*copied_out(n - 2))

            def transpose_rows(t, g):
                n = banks.index(("rows", t, g))
                bank_free(n)
                pe.wait_ge(gathered[t][g], 16 * len(GROUPS[g]))
                for s, k in enumerate(GROUPS[g]):
                    last = nc.tensor.transpose(featT[:, n % 2, s * P:(s + 1) * P], rows[:, t, k, :], ident[:, :])
                last.then_inc(featT_ready, 1)

            def gram_batch(t, half):
                batch = 2 * t + half
                if half == 0:
                    last_bank = banks.index(("rows", t, len(GROUPS) - 1))
                    pe.wait_ge(*copied_out(last_bank))
                    pe.wait_ge(*copied_out(last_bank - 1))
                if batch >= 1:
                    pe.wait_ge(pairs_done, 16 * batch)
                for q in range(HALF // 4):
                    s0 = HALF * half + 4 * q
                    last = nc.tensor.matmul(gram[:, q // 4, (q % 4) * 4 * COLS:(q % 4 + 1) * 4 * COLS],
                                            XT[:, t, s0:s0 + 4, :], XT[:, t, s0:s0 + 4, 0:COLS],
                                            start=True, stop=True)
                last.then_inc(gram_ready, 1)

            def layers(t):
                if t == 0:
                    pe.wait_ge(w1_loaded, 16 * 4)
                    pe.wait_ge(w1_summed, 1)
                else:
                    pe.wait_ge(h1_ready, t)
                pe.wait_ge(pairs_done, 32 * (t + 1))
                for m in range(H1 // P):
                    cols = slice(m * P, (m + 1) * P)
                    nc.tensor.matmul(ps1[:, m, :], w1s[:, cols], denseT[:, t, :], start=True, stop=False)
                    for c in range(CHUNKS):
                        k = P if c < CHUNKS - 1 else BIAS_ROW + 1
                        last = nc.tensor.matmul(ps1[:, m, :], w1p[0:k, c, cols], Z[0:k, c, t, :],
                                                start=False, stop=(c == CHUNKS - 1))
                last.then_inc(ps1_ready, 1)
                if t == 0:
                    pe.wait_ge(w2_loaded, 16 * 5)
                else:
                    pe.wait_ge(h2_ready, 2 * t)
                pe.wait_ge(h1_ready, t + 1)
                for m in range(H2 // P):
                    for c in range(H1 // P):
                        last = nc.tensor.matmul(ps2[:, m * P:(m + 1) * P], w2s[:, c, m * P:(m + 1) * P],
                                                h1[:, t % 2, c, :], start=(c == 0), stop=(c == H1 // P - 1))
                last.then_inc(ps2_ready, 1)
                pe.wait_ge(h2_ready, 2 * (t + 1))
                if t >= 1:
                    pe.wait_ge(y_ready, t)
                for c in range(H2 // P):
                    last = nc.tensor.matmul(ps3, w3s[:, c:c + 1], h2[:, t % 2, c, :],
                                            start=(c == 0), stop=(c == H2 // P - 1))
                last.then_inc(ps3_ready, 1)

            pe.wait_ge(consts_loaded, 32)
            pe.wait_ge(dense_loaded, 16)
            for t in range(TILES):
                last = nc.tensor.transpose(featT[:, 0, t * P:(t + 1) * P], dense_rows[:, t, :], ident[:, :])
            last.then_inc(featT_ready, 1)
            blocks = 0
            for i in range(n_onehot):
                n = 1 + i
                bank_free(n)
                pe.wait_ge(lo_ready, i + 1)
                r = rows_per_part[i]
                for c in range(r):
                    pe.wait_ge(onehot_ready, blocks + 1)
                    for part in (table_hi, table_lo):
                        last = nc.tensor.matmul(featT[:, n % 2, :], part[i % 2][0:PART, c, :],
                                                onehot[blocks % RING][0:PART, :],
                                                start=(c == 0 and part is table_hi),
                                                stop=(c == r - 1 and part is table_lo))
                    last.then_inc(onehot_used, 1)
                    blocks += 1
            for t in range(TILES):
                for g in range(len(GROUPS)):
                    if t == 0 or g >= 1:
                        transpose_rows(t, g)
                gram_batch(t, 0)
                if t + 1 < TILES:
                    transpose_rows(t + 1, 0)
                gram_batch(t, 1)
                layers(t)


def kernel(**inputs):
    import numpy as np
    import concourse.bacc as bacc
    from concourse.bass_utils import run_bass_kernel_spmd

    w1 = np.asarray(inputs["W_top1"])
    w1_pairs = np.zeros((P, CHUNKS, H1), w1.dtype)
    pair_mask = np.zeros((P, CHUNKS), np.int32)
    for k in range(PAIR_COLS):
        c, j = divmod(k, 4)
        for s in range(F):
            near = k + 1 <= s <= k + 13
            pair_mask[32 * j + s, c] = near and k < PAIR_COLS - 1
            if k == PAIR_COLS - 1:
                partner = F - 1 if s < PAIR_COLS - 1 else None
            else:
                partner = None if s == k else k if near else k + 13
            if partner is not None:
                a, b = sorted((FEATURE_OF_SLOT[s], FEATURE_OF_SLOT[partner]))
                w1_pairs[32 * j + s, c] = w1[D + a * F - a * (a + 1) // 2 + b - a - 1]
    w1_dense = np.concatenate([w1[0:D], w1[-D:]])
    ids = np.asarray(inputs["ids"])
    sizes = [inputs[f"tbl_{f}"].shape[0] // PART for f in ONEHOT]
    row_ids = np.zeros((P, 2, max(sizes)), np.float32)
    for w, r in enumerate((min(sizes), max(sizes))):
        row_ids[:, w, 0:r] = np.arange(P)[:, None] * r + np.arange(r)[None, :]

    nc = bacc.Bacc("TRN2", target_bir_lowering=False, num_devices=1)
    arrays = {}

    def given(name, a):
        arrays[name] = np.ascontiguousarray(a)
        return nc.dram_tensor(name, arrays[name].shape, mybir.dt.from_np(arrays[name].dtype),
                              kind="ExternalInput").ap()

    out = nc.dram_tensor("out_0", (B, 1), mybir.dt.float32, kind="ExternalOutput").ap()
    tower(
        nc,
        given("dense", inputs["r_dense_features"]),
        given("ids", ids),
        given("ids_by_table", ids.T[ONEHOT]),
        [given(f"tbl_{f}", inputs[f"tbl_{f}"]) for f in range(N_TABLES)],
        given("w1_pairs", w1_pairs),
        given("w1_dense", w1_dense),
        given("b1", inputs["b_top1"]),
        given("w2", inputs["W_top2"]),
        given("b2", inputs["b_top2"]),
        given("w3", inputs["W_top3"]),
        given("identity", np.eye(P, dtype=np.float32)),
        given("row_ids", row_ids),
        given("pair_mask", pair_mask),
        out,
    )
    result = run_bass_kernel_spmd(nc, [arrays], core_ids=[0])
    return result.results[0]["out_0"]
```

```python
import concourse.bass as bass
from concourse import mybir
from contextlib import ExitStack

B = 512
D = 128
N_TABLES = 26
F = N_TABLES + 1
P = 128
TILES = B // P
SLOTS = 32
COLS = 28
PAIR_COLS = (F + 1) // 2
CHUNKS = (PAIR_COLS + 3) // 4
H1, H2 = 512, 256
PART = 125
ONEHOT = [5, 9, 21, 22, 2, 3]
GATHERED = [f for f in range(N_TABLES) if f not in ONEHOT]
FEATURE_OF_SLOT = [0] + [f + 1 for f in ONEHOT] + [f + 1 for f in GATHERED]
SLOT_ONEHOT = 1
SLOT_GATHERED = 1 + len(ONEHOT)
GROUP = 4
GROUPS = [list(range(g, min(g + GROUP, len(GATHERED)))) for g in range(0, len(GATHERED), GROUP)]
BIAS_ROW = 64
ON_DVE = []
RING = 5
RING_ACT = 4


def by_act(rows, c):
    return c in (rows // 2, rows - 1)


LAST = TILES - 1
BATCH = 32
BATCHES = [(t, s) for t in range(TILES) for s in range(0, P, BATCH)]


def order():
    n, groups = len(ONEHOT), len(GROUPS)

    def rows(t, first, end=groups):
        return [x for g in range(first, min(end, groups)) for x in (("rows", t, g), ("out", "rows", t, g))]

    steps = [("split", 0), ("make", 0), ("out", "dense")]
    for i in range(n):
        steps += [("onehot", i)]
        if i + 1 < n:
            steps += [("split", i + 1), ("make", i + 1)]
        else:
            steps += [("weights", 0)]
        steps += [("out", "onehot", i)]
        if i >= 1:
            steps += rows(0, i - 1, i)
    steps += rows(0, n - 1)

    def pairs(b):
        return [("gram", b), ("pairs", b)]

    steps += [*pairs(0), *rows(1, 0, 1), ("weights", 1), *pairs(1), *rows(1, 1, 2), ("weights", 2),
              *pairs(2), *rows(1, 2, 3), *pairs(3), *rows(1, 3), ("parts", 0)]
    for t in range(1, LAST):
        steps += [*pairs(4 * t), *rows(t + 1, 0, 1)]
        if t == 1:
            steps += [("weights", 3)]
        steps += [*pairs(4 * t + 1)]
        if t == 1:
            steps += [("weights", 4)]
        steps += [("one", t - 1), *pairs(4 * t + 2), *rows(t + 1, 1, 2), ("hidden", t - 1), ("out", "hidden", t - 1),
                  *pairs(4 * t + 3), *rows(t + 1, 2, 3), ("two", t - 1), *rows(t + 1, 3), ("parts", t)]
    for b in range(4 * LAST, len(BATCHES)):
        steps += pairs(b)
    t = LAST - 1
    return steps + [("one", t), ("parts", LAST), ("hidden", t), ("out", "hidden", t), ("one", LAST), ("two", t),
                    ("hidden", LAST), ("out", "hidden", LAST), ("two", LAST)]


def tower(nc, dense, ids, ids_by_table, tables, w1_pairs, w1_dense, b1, w2, b2, w3, identity, row_ids,
          pair_mask, out):
    fp32, f32r, i32 = mybir.dt.float32, mybir.dt.float32r, mybir.dt.int32
    ALU, ACT = mybir.AluOpType, mybir.ActivationFunctionType
    n_onehot = len(ONEHOT)
    rows_per_part = [tables[f].shape[0] // PART for f in ONEHOT]
    max_rows = max(rows_per_part)

    with ExitStack() as ctx:
        def sb(name, shape, dt=fp32):
            return ctx.enter_context(nc.sbuf_tensor(name, shape, dt))

        def sem(name):
            return ctx.enter_context(nc.semaphore(name))

        index = sb("index", [P, TILES, N_TABLES], i32)
        onehot_ids = [sb(f"onehot_ids{i}", [P, B], i32) for i in range(3)]
        ident = sb("ident", [P, P])
        row_id = sb("row_id", [P, 4, max_rows])
        mask = sb("mask", [P, CHUNKS], i32)
        dense_rows = sb("dense_rows", [P, TILES, D])
        rows = sb("rows", [P, 2, len(GATHERED), D])
        XT = sb("XT", [P, TILES, P, SLOTS])
        tables_raw = sb("tables_raw", [P, 2 * max_rows * D])
        table = [tables_raw[:, i * max_rows * D:(i + 1) * max_rows * D].rearrange("p (r d) -> p r d", d=D)
                 for i in range(2)]
        table_hi = [sb(f"table_hi{i}", [P, max_rows, D], f32r) for i in range(2)]
        table_lo = [sb(f"table_lo{i}", [P, max_rows, D], f32r) for i in range(2)]
        onehot_dve = [sb(f"onehot_dve{i}", [P, B], f32r) for i in range(RING)]
        onehot_act = [sb(f"onehot_act{i}", [P, B], f32r) for i in range(RING_ACT)]
        distance = sb("distance", [P, B])
        Z = sb("Z", [P, CHUNKS, 2, P])
        w1_raw = tables_raw[:, 0:CHUNKS * H1].rearrange("p (c n) -> p c n", n=H1)
        w1d = sb("w1d", [P, 2, H1])
        w2s = sb("w2s", [P, H1 // P, H2])
        Zp = [sb(f"Z_{x}", [P, 2, CHUNKS, P], f32r) for x in "hl"]
        denseT = [sb(f"denseT_{x}", [P, TILES, P], f32r) for x in "hl"]
        w1p = [sb(f"w1p_{x}", [P, CHUNKS, H1], f32r) for x in "hl"]
        w1s = [sb(f"w1s_{x}", [P, H1], f32r) for x in "hl"]
        ones = sb("ones", [1, P])
        h1 = sb("h1", [P, H1])
        h1T = sb("h1T", [P, H1 // P, P])
        b2s = sb("b2s", [1, H2])
        w3s = sb("w3s", [P, H2])
        h2w = sb("h2w", [P, H2])
        y = sb("y", [P, TILES])

        gram = ctx.enter_context(nc.psum_tensor("gram", [P, 4, 512], fp32))
        featT = ctx.enter_context(nc.psum_tensor("featT", [P, 2, 512], fp32))
        ps1 = ctx.enter_context(nc.psum_tensor("ps1", [P, H1], fp32))
        ps2 = ctx.enter_context(nc.psum_tensor("ps2", [P, 512], fp32))[:, 0:H2]

        index_loaded = sem("index_loaded")
        row_id_loaded = sem("row_id_loaded")
        ident_loaded = sem("ident_loaded")
        mask_loaded = sem("mask_loaded")
        ids_loaded = [sem(f"ids_loaded{i}") for i in range(3)]
        dense_loaded = sem("dense_loaded")
        w1d_loaded = sem("w1d_loaded")
        w1_loaded = sem("w1_loaded")
        w2_loaded = sem("w2_loaded")
        table_loaded = [sem(f"table_loaded{i}") for i in range(2)]
        gathered = [[sem(f"gathered{t}_{g}") for g in range(len(GROUPS))] for t in range(TILES)]
        padded = sem("padded")
        w1_summed = sem("w1_summed")
        weights_hi = sem("weights_hi")
        weights_lo = sem("weights_lo")
        bias_row = sem("bias_row")
        hi_ready = sem("hi_ready")
        lo_ready = sem("lo_ready")
        onehot_ready = sem("onehot_ready")
        distance_ready = sem("distance_ready")
        onehot_ready_act = sem("onehot_ready_act")
        onehot_used = sem("onehot_used")
        featT_ready = sem("featT_ready")
        featT_act = sem("featT_act")
        featT_dve = sem("featT_dve")
        dense_hi = sem("dense_hi")
        dense_lo = sem("dense_lo")
        gram_ready = sem("gram_ready")
        base_copied = sem("base_copied")
        pairs_done = sem("pairs_done")
        Zhi_ready = sem("Zhi_ready")
        Zlo_ready = sem("Zlo_ready")
        ps1_ready = sem("ps1_ready")
        h1_ready = sem("h1_ready")
        ps2_ready = sem("ps2_ready")
        h2_ready = sem("h2_ready")
        ones_ready = sem("ones_ready")
        y_ready = sem("y_ready")
        stored = sem("stored")

        banks = [("dense",)] + [s for s in order() if s[0] in ("onehot", "rows", "hidden")]
        on_act = [b[0] != "rows" or b not in ON_DVE for b in banks]
        act_banks = [s[1:] for s in order() if s[0] == "out" and on_act[banks.index(s[1:])]]
        dve_banks = [s[1:] for s in order() if s[0] == "out" and not on_act[banks.index(s[1:])]]

        blocks = [(i, c) for i in range(n_onehot) for c in range(rows_per_part[i])]
        dve_blocks = [b for b in blocks if not by_act(rows_per_part[b[0]], b[1])]
        act_blocks = [b for b in blocks if by_act(rows_per_part[b[0]], b[1])]

        def written(bank):
            if bank[0] == "onehot":
                return onehot_used, sum(rows_per_part[:bank[1] + 1])
            return featT_ready, [b for b in banks if b[0] != "onehot"].index(bank) + 1

        def copied_out(bank):
            if bank in act_banks:
                return featT_act, act_banks.index(bank) + 1
            return featT_dve, dve_banks.index(bank) + 1

        def bank_to_XT(bank):
            src = featT[:, banks.index(bank) % 2, :]
            if bank[0] == "dense":
                return XT[:, :, :, 0], src.rearrange("d (t p) -> d t p", t=TILES)
            if bank[0] == "onehot":
                return XT[:, :, :, SLOT_ONEHOT + bank[1]], src.rearrange("d (p t) -> d t p", t=TILES)
            _, t, g = bank
            k = len(GROUPS[g])
            s = SLOT_GATHERED + GROUPS[g][0]
            return (XT[:, t, :, s:s + k].rearrange("d p s -> d s p"),
                    src[:, 0:k * P].rearrange("d (s p) -> d s p", s=k))

        def pair_block(batch, i, j, first, count):
            t, s0 = BATCHES[batch]
            bank = 2 * (batch % 2)
            src = gram[32 * i:32 * i + 32, bank:bank + 2, 0:4 * 4 * COLS]
            at = COLS * i + first
            src = src.rearrange("p b (q c) -> p b q c", q=4)[:, :, :, at:at + 4 * (count - 1) + 1:4]
            dst = Z[32 * j:32 * j + 32, 0:count, t % 2, s0:s0 + BATCH]
            dst = dst.rearrange("p k (b q i) -> p b q k i", b=2, q=4)[:, :, :, :, i]
            return dst, src

        def pairs_of(t):
            return 16 * sum(b[0] <= t for b in BATCHES)

        tail = slice(0, BIAS_ROW + 1)
        weights = [((w1_summed, 1), w1s[0][:, :], w1s[1][:, :], w1d[:, 0, :])]
        weights += [((w1_loaded, 16 * 3), w1p[0][:, c, :], w1p[1][:, c, :], w1_raw[:, c, :])
                    for c in range(CHUNKS - 1)]
        weights += [((w1_loaded, 16 * 3), w1p[0][tail, CHUNKS - 1, :], w1p[1][tail, CHUNKS - 1, :],
                     w1_raw[tail, CHUNKS - 1, :])]

        block = ctx.enter_context(nc.Block())

        @block.sync
        def _(sp):
            def load_table(i):
                r = rows_per_part[i]
                if i >= 3:
                    sp.wait_ge(onehot_ready, sum(b[0] <= i - 3 for b in dve_blocks))
                    sp.wait_ge(onehot_ready_act, sum(b[0] <= i - 3 for b in act_blocks))
                sp.dma_start(onehot_ids[i % 3][0:PART, :],
                             ids_by_table[i:i + 1, :].to_broadcast([PART, B])).then_inc(ids_loaded[i % 3], 16)
                if i >= 2:
                    sp.wait_ge(hi_ready, i - 1)
                    sp.wait_ge(lo_ready, i - 1)
                sp.dma_start(table[i % 2][0:PART, 0:r, :],
                             tables[ONEHOT[i]].rearrange("(p r) d -> p r d", r=r)).then_inc(table_loaded[i % 2], 16)

            sp.dma_start(index[:, :, :], ids.rearrange("(p t) f -> p t f", t=TILES)).then_inc(index_loaded, 16)
            sp.dma_start(row_id[:, :, :], row_ids).then_inc(row_id_loaded, 16)
            load_table(0)
            sp.dma_start(ident[:, :], identity).then_inc(ident_loaded, 16)
            sp.dma_start(dense_rows[:, :, :], dense.rearrange("(p t) d -> p t d", t=TILES)).then_inc(dense_loaded, 16)
            load_table(1)
            sp.dma_start(mask[:, :], pair_mask).then_inc(mask_loaded, 16)
            load_table(2)
            sp.dma_start(w1d[:, :, :], w1_dense.rearrange("(c p) n -> p c n", c=2)).then_inc(w1d_loaded, 16)
            sp.dma_start(w2s[:, :, :], w2.rearrange("(c p) n -> p c n", p=P)).then_inc(w2_loaded, 16)
            sp.dma_start(b2s[:, :], b2.unsqueeze(0)).then_inc(w2_loaded, 16)
            sp.dma_start(w3s[:, :], w3.rearrange("n o -> o n").to_broadcast([P, H2])).then_inc(w2_loaded, 16)
            for i in range(3, n_onehot):
                load_table(i)
            sp.wait_ge(hi_ready, n_onehot)
            sp.wait_ge(lo_ready, n_onehot)
            sp.dma_start(w1_raw[:, 0:CHUNKS - 1, :], w1_pairs[:, 0:CHUNKS - 1, :]).then_inc(w1_loaded, 16)
            sp.dma_start(w1_raw[0:BIAS_ROW, CHUNKS - 1, :], w1_pairs[0:BIAS_ROW, CHUNKS - 1, :]).then_inc(w1_loaded, 16)
            sp.dma_start(w1_raw[BIAS_ROW:BIAS_ROW + 1, CHUNKS - 1, :], b1.unsqueeze(0)).then_inc(w1_loaded, 16)
            sp.wait_ge(y_ready, TILES)
            sp.dma_start(out.rearrange("(p t) n -> p (t n)", t=TILES), y[:, :]).then_inc(stored, 16)
            sp.wait_ge(stored, 16)

        @block.gpsimd
        def _(pool):
            pool.wait_ge(index_loaded, 16)
            for t in range(TILES):
                for g, group in enumerate(GROUPS):
                    if t >= 2:
                        pool.wait_ge(*written(("rows", t - 2, g)))
                    for k in group:
                        f = GATHERED[k]
                        pool.indirect_dma_start(
                            rows[:, t % 2, k, :], None, tables[f],
                            bass.IndirectOffsetOnAxis(ap=index[:, t, f:f + 1], axis=0),
                        ).then_inc(gathered[t][g], 16)

        @block.scalar
        def _(act):
            def copy(dst, src):
                return nc.scalar.activation(dst, src, ACT.Copy)

            for step, *a in order():
                if step == "split":
                    i, = a
                    r = rows_per_part[i]
                    act.wait_ge(table_loaded[i % 2], 16 * (i // 2 + 1))
                    if i >= 2:
                        act.wait_ge(*written(("onehot", i - 2)))
                    copy(table_hi[i % 2][0:PART, 0:r, :], table[i % 2][0:PART, 0:r, :]).then_inc(hi_ready, 1)
                elif step == "make":
                    i, = a
                    act.wait_ge(row_id_loaded, 16)
                    act.wait_ge(ids_loaded[i % 3], 16 * (i // 3 + 1))
                    for n, (_, c) in enumerate(act_blocks):
                        if act_blocks[n][0] != i:
                            continue
                        if n:
                            act.wait_ge(onehot_ready_act, n)
                        nc.scalar.activation(distance[0:PART, :], onehot_ids[i % 3][0:PART, :], ACT.Abs,
                                             bias=row_id[0:PART, 2 + int(rows_per_part[i] == max_rows), c:c + 1],
                                             ).then_inc(distance_ready, 1)
                        act.wait_ge(distance_ready, n + 1)
                        if n >= RING_ACT:
                            act.wait_ge(onehot_used, blocks.index(act_blocks[n - RING_ACT]) + 1)
                        nc.scalar.activation(onehot_act[n % RING_ACT][0:PART, :], distance[0:PART, :], ACT.Relu,
                                             bias=1.0, scale=-1.0).then_inc(onehot_ready_act, 1)
                elif step == "out" and a[0] == "hidden":
                    bank = tuple(a)
                    act.wait_ge(*written(bank))
                    if a[1] >= 1:
                        act.wait_ge(ps2_ready, a[1])
                    src = featT[:, banks.index(bank) % 2, :].rearrange("n (c p) -> n c p", p=P)
                    copy(h1T[:, :, :], src).then_inc(featT_act, 1)
                elif step == "out" and tuple(a) in act_banks:
                    act.wait_ge(*written(tuple(a)))
                    dst, src = bank_to_XT(tuple(a))
                    if a[0] == "dense":
                        copy(denseT[0][:, :, :], src).then_inc(dense_hi, 1)
                    copy(dst, src).then_inc(featT_act, 1)
                elif step == "weights":
                    piece, = a
                    act.wait_ge(*weights[piece][0])
                    _, high, _, raw = weights[piece]
                    copy(high, raw).then_inc(weights_hi, 1)
                elif step == "pairs":
                    batch, = a
                    t = BATCHES[batch][0]
                    if t >= 2:
                        act.wait_ge(Zlo_ready, t - 1)
                    act.wait_ge(gram_ready, batch + 1)
                    for i in range(4):
                        for j in range(4):
                            count = len(range(j, PAIR_COLS, 4))
                            dst, src = pair_block(batch, i, j, PAIR_COLS - 1 + j, count)
                            copy(dst, src).then_inc(base_copied, 1)
                elif step == "one":
                    t, = a
                    act.wait_ge(ps1_ready, t + 1)
                    if t >= 1:
                        act.wait_ge(*written(("hidden", t - 1)))
                    nc.scalar.activation(h1[:, :], ps1[:, :], ACT.Relu).then_inc(h1_ready, 1)

        @block.vector
        def _(dve):
            def low(dst, whole, high):
                return nc.vector.tensor_tensor(dst, whole, high.bitcast(fp32), ALU.subtract)

            nc.vector.memset(XT[:, :, :, F:SLOTS], 0.0).then_inc(padded, 1)
            nc.vector.memset(Z[BIAS_ROW:P, CHUNKS - 1, :, :], 1.0).then_inc(bias_row, 1)
            nc.vector.memset(ones[:, :], 1.0).then_inc(ones_ready, 1)
            dve.wait_ge(row_id_loaded, 16)
            for step, *a in order():
                if step == "split":
                    i, = a
                    r = rows_per_part[i]
                    dve.wait_ge(hi_ready, i + 1)
                    if i >= 2:
                        dve.wait_ge(*written(("onehot", i - 2)))
                    low(table_lo[i % 2][0:PART, 0:r, :], table[i % 2][0:PART, 0:r, :],
                        table_hi[i % 2][0:PART, 0:r, :]).then_inc(lo_ready, 1)
                elif step == "make":
                    i, = a
                    r = rows_per_part[i]
                    dve.wait_ge(ids_loaded[i % 3], 16 * (i // 3 + 1))
                    for n, (_, c) in enumerate(dve_blocks):
                        if dve_blocks[n][0] != i:
                            continue
                        if n >= RING:
                            dve.wait_ge(onehot_used, blocks.index(dve_blocks[n - RING]) + 1)
                        nc.vector.tensor_scalar(onehot_dve[n % RING][0:PART, :], onehot_ids[i % 3][0:PART, :],
                                                row_id[0:PART, int(r == max_rows), c:c + 1], None,
                                                ALU.is_equal).then_inc(onehot_ready, 1)
                elif step == "out" and a[0] == "dense":
                    dve.wait_ge(dense_hi, 1)
                    dve.wait_ge(featT_act, 1)
                    low(denseT[1][:, :, :], featT[:, 0, :].rearrange("d (t p) -> d t p", t=TILES),
                        denseT[0][:, :, :]).then_inc(dense_lo, 1)
                elif step == "out" and tuple(a) in dve_banks:
                    dve.wait_ge(*written(tuple(a)))
                    nc.vector.tensor_copy(*bank_to_XT(tuple(a))).then_inc(featT_dve, 1)
                elif step == "weights":
                    piece, = a
                    if piece == 0:
                        dve.wait_ge(w1d_loaded, 16)
                        nc.vector.tensor_tensor(w1d[:, 0, :], w1d[:, 0, :], w1d[:, 1, :],
                                                ALU.add).then_inc(w1_summed, 1)
                    dve.wait_ge(weights_hi, piece + 1)
                    _, high, lo, raw = weights[piece]
                    low(lo, raw, high).then_inc(weights_lo, 1)
                elif step == "pairs":
                    batch, = a
                    if batch == 0:
                        dve.wait_ge(mask_loaded, 16)
                    for i in range(4):
                        dve.wait_ge(base_copied, 16 * batch + 4 * (i + 1))
                        for j in range(4):
                            count = len(range(j, PAIR_COLS - 1, 4))
                            dst, src = pair_block(batch, i, j, j, count)
                            m = mask[32 * j:32 * j + 32, 0:count].unsqueeze(1).unsqueeze(1)
                            nc.vector.copy_predicated(dst, m.to_broadcast([32, 2, 4, count]),
                                                      src).then_inc(pairs_done, 1)
                elif step == "parts":
                    t, = a
                    whole = Z[:, :, t % 2, :]
                    if t == 0:
                        dve.wait_ge(bias_row, 1)
                    dve.wait_ge(pairs_done, pairs_of(t))
                    if t >= 2:
                        dve.wait_ge(ps1_ready, t - 1)
                    nc.vector.tensor_copy(Zp[0][:, t % 2, :, :], whole).then_inc(Zhi_ready, 1)
                    dve.wait_ge(Zhi_ready, t + 1)
                    low(Zp[1][:, t % 2, :, :], whole, Zp[0][:, t % 2, :, :]).then_inc(Zlo_ready, 1)
                elif step == "two":
                    t, = a
                    dve.wait_ge(ps2_ready, t + 1)
                    if t >= 1:
                        dve.wait_ge(y_ready, t)
                    nc.vector.scalar_tensor_tensor(h2w[:, :], ps2, 0.0, w3s[:, :], ALU.max,
                                                   ALU.mult).then_inc(h2_ready, 1)
                    dve.wait_ge(h2_ready, t + 1)
                    nc.vector.reduce_sum(y[:, t:t + 1], h2w[:, :], mybir.AxisListType.X).then_inc(y_ready, 1)

        @block.tensor
        def _(pe):
            def bank_free(bank):
                n = banks.index(bank)
                if n >= 2:
                    pe.wait_ge(*copied_out(banks[n - 2]))
                if n == 2:
                    pe.wait_ge(dense_lo, 1)

            def product(dst, x, w, first, last):
                for n, (i, j) in enumerate(((0, 0), (0, 1), (1, 0))):
                    mm = nc.tensor.matmul(dst, x[i], w[j], start=first and n == 0, stop=last and n == 2)
                return mm

            pe.wait_ge(ident_loaded, 16)
            pe.wait_ge(dense_loaded, 16)
            for t in range(TILES):
                last = nc.tensor.transpose(featT[:, 0, t * P:(t + 1) * P], dense_rows[:, t, :], ident[:, :])
            last.then_inc(featT_ready, 1)
            for step, *a in order():
                if step == "onehot":
                    i, = a
                    n = banks.index(("onehot", i))
                    bank_free(("onehot", i))
                    pe.wait_ge(hi_ready, i + 1)
                    pe.wait_ge(lo_ready, i + 1)
                    r = rows_per_part[i]
                    for c in range(r):
                        if by_act(r, c):
                            m = act_blocks.index((i, c))
                            pe.wait_ge(onehot_ready_act, m + 1)
                            x = onehot_act[m % RING_ACT]
                        else:
                            m = dve_blocks.index((i, c))
                            pe.wait_ge(onehot_ready, m + 1)
                            x = onehot_dve[m % RING]
                        for part in (table_hi, table_lo):
                            last = nc.tensor.matmul(featT[:, n % 2, :], part[i % 2][0:PART, c, :], x[0:PART, :],
                                                    start=(c == 0 and part is table_hi),
                                                    stop=(c == r - 1 and part is table_lo))
                        last.then_inc(onehot_used, 1)
                elif step == "rows":
                    t, g = a
                    n = banks.index(("rows", t, g))
                    bank_free(("rows", t, g))
                    pe.wait_ge(gathered[t][g], 16 * len(GROUPS[g]))
                    for s, k in enumerate(GROUPS[g]):
                        last = nc.tensor.transpose(featT[:, n % 2, s * P:(s + 1) * P], rows[:, t % 2, k, :],
                                                   ident[:, :])
                    last.then_inc(featT_ready, 1)
                elif step == "gram":
                    batch, = a
                    t, s0 = BATCHES[batch]
                    bank = 2 * (batch % 2)
                    pe.wait_ge(padded, 1)
                    for b in (("onehot", n_onehot - 1), ("rows", t, len(GROUPS) - 2), ("rows", t, len(GROUPS) - 1)):
                        pe.wait_ge(*copied_out(b))
                    if batch >= 2:
                        pe.wait_ge(pairs_done, 16 * (batch - 1))
                    for q in range(BATCH // 4):
                        s = s0 + 4 * q
                        last = nc.tensor.matmul(gram[:, bank + q // 4, q % 4 * 4 * COLS:(q % 4 + 1) * 4 * COLS],
                                                XT[:, t, s:s + 4, :], XT[:, t, s:s + 4, 0:COLS],
                                                start=True, stop=True)
                    last.then_inc(gram_ready, 1)
                elif step == "one":
                    t, = a
                    if t == 0:
                        pe.wait_ge(weights_lo, len(weights))
                        pe.wait_ge(dense_lo, 1)
                    else:
                        pe.wait_ge(h1_ready, t)
                    product(ps1[:, :], [x[:, t, :] for x in denseT], [w[:, :] for w in w1s], True, False)
                    pe.wait_ge(Zlo_ready, t + 1)
                    for c in range(CHUNKS):
                        k = P if c < CHUNKS - 1 else BIAS_ROW + 1
                        last = product(ps1[:, :], [x[0:k, t % 2, c, :] for x in Zp], [w[0:k, c, :] for w in w1p],
                                       False, c == CHUNKS - 1)
                    last.then_inc(ps1_ready, 1)
                elif step == "hidden":
                    t, = a
                    n = banks.index(("hidden", t))
                    bank_free(("hidden", t))
                    pe.wait_ge(h1_ready, t + 1)
                    for c in range(H1 // P):
                        last = nc.tensor.transpose(featT[:, n % 2, c * P:(c + 1) * P], h1[:, c * P:(c + 1) * P],
                                                   ident[:, :])
                    last.then_inc(featT_ready, 1)
                elif step == "two":
                    t, = a
                    if t == 0:
                        pe.wait_ge(ones_ready, 1)
                        pe.wait_ge(w2_loaded, 16 * 3)
                    else:
                        pe.wait_ge(h2_ready, t)
                    nc.tensor.matmul(ps2, ones[:, :], b2s[:, :], start=True, stop=False)
                    pe.wait_ge(*copied_out(("hidden", t)))
                    for c in range(H1 // P):
                        last = nc.tensor.matmul(ps2, h1T[:, c, :], w2s[:, c, :], start=False,
                                                stop=c == H1 // P - 1)
                    last.then_inc(ps2_ready, 1)


def kernel(**inputs):
    import numpy as np
    import concourse.bacc as bacc
    from concourse.bass_utils import run_bass_kernel_spmd

    w1 = np.asarray(inputs["W_top1"])
    w1_pairs = np.zeros((P, CHUNKS, H1), w1.dtype)
    pair_mask = np.zeros((P, CHUNKS), np.int32)
    for k in range(PAIR_COLS):
        c, j = divmod(k, 4)
        for s in range(F):
            near = k + 1 <= s <= k + 13
            pair_mask[32 * j + s, c] = near and k < PAIR_COLS - 1
            if k == PAIR_COLS - 1:
                partner = F - 1 if s < PAIR_COLS - 1 else None
            else:
                partner = None if s == k else k if near else k + 13
            if partner is not None:
                a, b = sorted((FEATURE_OF_SLOT[s], FEATURE_OF_SLOT[partner]))
                w1_pairs[32 * j + s, c] = w1[D + a * F - a * (a + 1) // 2 + b - a - 1]
    w1_dense = np.concatenate([w1[0:D], w1[-D:]])
    ids = np.asarray(inputs["ids"])
    sizes = [inputs[f"tbl_{f}"].shape[0] // PART for f in ONEHOT]
    row_ids = np.zeros((P, 4, max(sizes)), np.float32)
    for w, r in enumerate((min(sizes), max(sizes))):
        row_ids[:, w, 0:r] = np.arange(P)[:, None] * r + np.arange(r)[None, :]
        row_ids[:, 2 + w, 0:r] = -row_ids[:, w, 0:r]

    nc = bacc.Bacc("TRN2", target_bir_lowering=False, num_devices=1)
    arrays = {}

    def given(name, a):
        arrays[name] = np.ascontiguousarray(a)
        return nc.dram_tensor(name, arrays[name].shape, mybir.dt.from_np(arrays[name].dtype),
                              kind="ExternalInput").ap()

    out = nc.dram_tensor("out_0", (B, 1), mybir.dt.float32, kind="ExternalOutput").ap()
    tower(
        nc,
        given("dense", inputs["r_dense_features"]),
        given("ids", ids),
        given("ids_by_table", ids.T[ONEHOT]),
        [given(f"tbl_{f}", inputs[f"tbl_{f}"]) for f in range(N_TABLES)],
        given("w1_pairs", w1_pairs),
        given("w1_dense", w1_dense),
        given("b1", inputs["b_top1"]),
        given("w2", inputs["W_top2"]),
        given("b2", inputs["b_top2"]),
        given("w3", inputs["W_top3"]),
        given("identity", np.eye(P, dtype=np.float32)),
        given("row_ids", row_ids),
        given("pair_mask", pair_mask),
        out,
    )
    result = run_bass_kernel_spmd(nc, [arrays], core_ids=[0])
    return result.results[0]["out_0"]
```

```python
import concourse.bass as bass
from concourse import mybir
from contextlib import ExitStack

B = 512
D = 128
N_TABLES = 26
F = N_TABLES + 1
P = 128
TILES = B // P
SLOTS = 32
REPEATS = {8: [27, 28], 17: [29], 26: [30], 22: [31]}
COLS = 28
PAIR_COLS = 12
CHUNKS = PAIR_COLS // 4
H1, H2 = 512, 256
PART = 125
ONEHOT = [5, 9, 21, 22, 2, 3, 4]
PARTLY, PARTLY_FROM = 6, 2
GATHERED = [f for f in range(N_TABLES) if f not in ONEHOT + [PARTLY]] + [PARTLY]
SLOT_DENSE = 26
SLOTS_ONEHOT = [17, 8, 22, 21, 23, 24, 25]
SLOTS_GATHERED = [s for s in range(F) if s not in SLOTS_ONEHOT + [SLOT_DENSE]]
FEATURE_OF_SLOT = {SLOT_DENSE: 0}
FEATURE_OF_SLOT.update({s: f + 1 for s, f in zip(SLOTS_ONEHOT, ONEHOT)})
FEATURE_OF_SLOT.update({s: f + 1 for s, f in zip(SLOTS_GATHERED, GATHERED)})
GROUP = 4
GROUPS = [list(range(g, min(g + GROUP, len(GATHERED)))) for g in range(0, len(GATHERED), GROUP)]


def group(t, g):
    return [k for k in GROUPS[g] if t < PARTLY_FROM or GATHERED[k] != PARTLY]


BIAS_ROW = P - 1
WARM_UP = 12
RING = 9
RING_ACT = 3
LAST = TILES - 1
BATCH = 32
BATCHES = [(t, s) for t in range(TILES) for s in range(0, P, BATCH)]
PAIR_COPIES = 20
PARTS_POOL = [(0, 64), (64, 96)]
PIECES = [(t, 0, H1) for t in range(LAST)] + [(LAST, 0, H1 // 2), (LAST, H1 // 2, H1)]

SCHEDULE = [
    "gram0 weights1 next0 next_out0 gram1 next1 next2 next_out1 weights2 next_out2 gram2 "
    "next3 next_out3 next4 next_out4 weights3 gram3 parts",
    "gram0 next0 next_out0 split gram1 make0 prev_one prev_relu next1 next_out1 prev_bias "
    "gram2 next2 next_out2 prev_hidden make1 gram3 lookup next3 next_out3 prev_two parts "
    "next4 next_out4",
    "gram0 next0 next_out0 prev_bias prev_one prev_relu gram1 gram2 prev_hidden next1 gram3 "
    "next_out1 parts prev_two next2 next_out2",
    "rows3 prev_one rows4 rows_out3 rows_out4 prev_relu gram0 prev_hidden gram1 gram2 gram3 "
    "parts prev_bias prev_two one0 one1 hidden0 bias hidden1 two",
]


def rows_of(j):
    return 31 if j == 3 else 32


def made_first(i):
    return 6 if i == 0 else 4


def by_act(rows, c):
    return c == rows - 1 or rows > 8 and c == rows // 2


def order():
    n = len(ONEHOT)
    steps = [("make", 0, 0), ("split", 0), ("make", 0, 1)]
    for i in range(n):
        steps += [("onehot", i)]
        if i == 0:
            steps += [("dense",)]
        if i + 1 < n:
            steps += [("make", i + 1, 0), ("split", i + 1), ("make", i + 1, 1)]
        else:
            steps += [("weights", 0)]
        if i == 0:
            steps += [("out", "dense")]
        steps += [("out", "onehot", i)]
        if 1 <= i <= len(GROUPS):
            steps += [("rows", 0, i - 1), ("out", "rows", 0, i - 1)]
    for t, words in enumerate(SCHEDULE):
        for word in words.split():
            name, x = word.rstrip("0123456789"), int(word[-1]) if word[-1].isdigit() else 0
            steps += {
                "gram": [("gram", 4 * t + x), ("pairs", 4 * t + x)],
                "parts": [("parts", t)],
                "rows": [("rows", t, x)],
                "rows_out": [("out", "rows", t, x)],
                "next": [("rows", t + 1, x)],
                "next_out": [("out", "rows", t + 1, x)],
                "weights": [("weights", x)],
                "split": [("split", n)],
                "make": [("make", n, x)],
                "lookup": [("onehot", n), ("out", "onehot", n)],
                "prev_one": [("one", t - 1)],
                "prev_relu": [("relu", t - 1)],
                "prev_hidden": [("hidden", t - 1), ("out", "hidden", t - 1)],
                "prev_bias": [("bias", t - 1)],
                "prev_two": [("two", t - 1)],
                "one": [("one", t + x), ("relu", t + x)],
                "hidden": [("hidden", t + x), ("out", "hidden", t + x)],
                "bias": [("bias", t)],
                "two": [("two", t)],
            }[name]
    return steps


def tower(nc, dense, ids, ids_by_table, tables, w1_pairs, w1_dense, w2, b2, w3, identity, row_ids,
          pair_mask, out):
    fp32, f32r, i32 = mybir.dt.float32, mybir.dt.float32r, mybir.dt.int32
    ALU, ACT = mybir.AluOpType, mybir.ActivationFunctionType
    n_onehot = len(ONEHOT)
    rows_per_part = [tables[f].shape[0] // PART for f in ONEHOT + [PARTLY]]
    max_rows = max(rows_per_part)

    with ExitStack() as ctx:
        def sb(name, shape, dt=fp32):
            return ctx.enter_context(nc.sbuf_tensor(name, shape, dt))

        def sem(name):
            return ctx.enter_context(nc.semaphore(name))

        index = sb("index", [P, TILES, N_TABLES], i32)
        onehot_ids = [sb(f"onehot_ids{i}", [P, B], i32) for i in range(3)]
        ident = sb("ident", [P, P])
        row_id = sb("row_id", [P, 4, max_rows])
        mask = sb("mask", [P, 2, CHUNKS], i32)
        dense_rows = sb("dense_rows", [P, TILES, D])
        rows = sb("rows", [P, 2, len(GATHERED), D])
        XT = sb("XT", [P, TILES, P, SLOTS])
        tables_raw = sb("tables_raw", [P, 2 * max_rows * D])
        table = [tables_raw[:, i * max_rows * D:(i + 1) * max_rows * D].rearrange("p (r d) -> p r d", d=D)
                 for i in range(2)]
        table_hi = [sb(f"table_hi{i}", [P, max_rows, D], f32r) for i in range(2)]
        table_lo = [sb(f"table_lo{i}", [P, max_rows, D], f32r) for i in range(2)]
        onehot_dve = [sb(f"onehot_dve{i}", [P, B], f32r) for i in range(RING)]
        onehot_act = [sb(f"onehot_act{i}", [P, B], f32r) for i in range(RING_ACT)]
        distance = sb("distance", [P, B])
        Z = sb("Z", [P, CHUNKS, 2, P])
        w1_raw = sb("w1_raw", [P, CHUNKS, H1])
        w1d = sb("w1d", [P, 2, H1])
        w2s = sb("w2s", [P, H1 // P, H2])
        Zp = [sb(f"Z_{x}", [P, 2, CHUNKS, P], f32r) for x in "hl"]
        denseT = [sb(f"denseT_{x}", [P, TILES, P], f32r) for x in "hl"]
        w1p = [sb(f"w1p_{x}", [P, CHUNKS, H1], f32r) for x in "hl"]
        w1s = [sb(f"w1s_{x}", [P, H1], f32r) for x in "hl"]
        ones = sb("ones", [P, P])
        h1 = sb("h1", [P, 2, H1])
        h1T = sb("h1T", [P, H1 // P, P])
        b2s = sb("b2s", [1, H2])
        w3s = sb("w3s", [P, H2])
        h2w = sb("h2w", [P, H2])
        y = sb("y", [P, TILES])

        psum = ctx.enter_context(nc.psum_tensor("psum", [P, 8, 512], fp32))
        gram, featT = psum[:, 0:4, :], psum[:, 4:6, :]
        ps1 = [psum[:, 6, :]] * LAST
        ps1 += [gram[:, 2 + half, 0:H1 // 2] for half in range(2)]
        ps2 = psum[:, 7, 0:H2]

        index_loaded = sem("index_loaded")
        row_id_loaded = sem("row_id_loaded")
        ident_loaded = sem("ident_loaded")
        mask_loaded = sem("mask_loaded")
        ids_loaded = [sem(f"ids_loaded{i}") for i in range(3)]
        dense_loaded = sem("dense_loaded")
        w1d_loaded = sem("w1d_loaded")
        w1_loaded = sem("w1_loaded")
        w2_loaded = sem("w2_loaded")
        table_loaded = [sem(f"table_loaded{i}") for i in range(2)]
        gathered = [[sem(f"gathered{t}_{g}") for g in range(len(GROUPS))] for t in range(TILES)]
        w1_summed = sem("w1_summed")
        weights_hi = sem("weights_hi")
        weights_lo = sem("weights_lo")
        bias_row = sem("bias_row")
        hi_ready = sem("hi_ready")
        lo_ready = sem("lo_ready")
        onehot_ready = sem("onehot_ready")
        distance_ready = sem("distance_ready")
        onehot_ready_act = sem("onehot_ready_act")
        onehot_used = sem("onehot_used")
        featT_ready = sem("featT_ready")
        featT_act = sem("featT_act")
        dense_hi = sem("dense_hi")
        dense_lo = sem("dense_lo")
        gram_ready = sem("gram_ready")
        base_copied = sem("base_copied")
        pairs_done = sem("pairs_done")
        Zhi_ready = sem("Zhi_ready")
        Zlo_ready = sem("Zlo_ready")
        Zhi_pool = sem("Zhi_pool")
        Zlo_pool = sem("Zlo_pool")
        ps1_ready = sem("ps1_ready")
        h1_ready = sem("h1_ready")
        ps2_ready = sem("ps2_ready")
        h2_ready = sem("h2_ready")
        ones_ready = sem("ones_ready")
        y_ready = sem("y_ready")
        stored = sem("stored")

        banks = [("dense",)] + [s for s in order() if s[0] in ("rows", "hidden") or s == ("onehot", n_onehot)]
        copied = [s[1:] for s in order() if s[0] == "out"]

        blocks = [(i, c) for i in range(n_onehot + 1) for c in range(rows_per_part[i])]
        dve_blocks = [b for b in blocks if not by_act(rows_per_part[b[0]], b[1])]
        act_blocks = [b for b in blocks if by_act(rows_per_part[b[0]], b[1])]

        def block(ring, i):
            return ring[0:PART, 0:B if i < n_onehot else (TILES - PARTLY_FROM) * P]

        def ids_of(i):
            ids = onehot_ids[i % 3][0:PART, :]
            if i < n_onehot:
                return ids
            return ids.rearrange("c (p t) -> c t p", t=TILES)[:, PARTLY_FROM:TILES, :]

        def as_ids(block, i):
            return block if i < n_onehot else block.rearrange("c (t p) -> c t p", p=P)

        def written(bank):
            if bank[0] == "onehot" and bank[1] < n_onehot:
                return onehot_used, sum(rows_per_part[:bank[1] + 1])
            return featT_ready, banks.index(bank) + 1

        def copied_out(bank):
            return featT_act, copied.index(bank) + 1

        def bank_to_XT(bank):
            if bank == ("onehot", n_onehot):
                src = featT[:, banks.index(bank) % 2, 0:(TILES - PARTLY_FROM) * P]
                return (XT[:, PARTLY_FROM:TILES, :, SLOTS_GATHERED[-1]], src.rearrange("d (t p) -> d t p", p=P))
            if bank[0] == "onehot":
                src = gram[:, bank[1] % 4, :]
                return XT[:, :, :, SLOTS_ONEHOT[bank[1]]], src.rearrange("d (p t) -> d t p", t=TILES)
            src = featT[:, banks.index(bank) % 2, :]
            if bank[0] == "dense":
                return XT[:, :, :, SLOT_DENSE], src.rearrange("d (t p) -> d t p", t=TILES)
            _, t, g = bank
            k = len(group(t, g))
            s = SLOTS_GATHERED[GROUPS[g][0]]
            return (XT[:, t, :, s:s + k].rearrange("d p s -> d s p"),
                    src[:, 0:k * P].rearrange("d (s p) -> d s p", s=k))

        def repeats_of(bank):
            slot = SLOT_DENSE if bank[0] == "dense" else None
            if bank[0] == "onehot" and bank[1] < n_onehot:
                slot = SLOTS_ONEHOT[bank[1]]
            return [(XT[:, :, :, s], bank_to_XT(bank)[1]) for s in REPEATS.get(slot, [])]

        def gram_bank(batch):
            return 4 if batch == len(BATCHES) - 2 else 0 if batch == len(BATCHES) - 1 else 2 * (batch % 2)

        def pair_block(batch, i, j, first):
            t, s0 = BATCHES[batch]
            bank, n = gram_bank(batch), rows_of(j)
            src = psum[32 * i:32 * i + n, bank:bank + 2, :].rearrange("p b (q c) -> p (b q) c", q=4)
            src = src[:, :, COLS * i:COLS * i + F].rearrange("p g (m x) -> p g x m", m=CHUNKS)
            src = src[:, :, first, :]
            dst = Z[32 * j:32 * j + n, :, t % 2, s0:s0 + BATCH]
            dst = dst.rearrange("p m (g i) -> p g m i", i=4)[:, :, :, i]
            return dst, src

        def pairs_of(t):
            return PAIR_COPIES * sum(b[0] <= t for b in BATCHES)

        weights = [((w1_summed, 1), w1s[0][:, :], w1s[1][:, :], w1d[:, 0, :])]
        weights += [((w1_loaded, 16), w1p[0][:, c, :], w1p[1][:, c, :], w1_raw[:, c, :])
                    for c in range(CHUNKS)]

        program = ctx.enter_context(nc.Block())

        @program.sync
        def _(sp):
            def load_ids(i):
                if i >= 3:
                    sp.wait_ge(onehot_ready, sum(b[0] <= i - 3 for b in dve_blocks))
                    sp.wait_ge(onehot_ready_act, sum(b[0] <= i - 3 for b in act_blocks))
                sp.dma_start(onehot_ids[i % 3][0:PART, :],
                             ids_by_table[i:i + 1, :].to_broadcast([PART, B])).then_inc(ids_loaded[i % 3], 16)

            def load_table(i):
                r = rows_per_part[i]
                if i >= 2:
                    sp.wait_ge(hi_ready, i - 1)
                    sp.wait_ge(lo_ready, i - 1)
                sp.dma_start(table[i % 2][0:PART, 0:r, :],
                             tables[(ONEHOT + [PARTLY])[i]].rearrange("(p r) d -> p r d", r=r),
                             ).then_inc(table_loaded[i % 2], 16)

            sp.dma_start(index[:, :, :], ids.rearrange("(p t) f -> p t f", t=TILES)).then_inc(index_loaded, 16)
            sp.dma_start(row_id[:, :, :], row_ids).then_inc(row_id_loaded, 16)
            load_ids(0)
            load_table(0)
            load_ids(1)
            load_table(1)
            sp.dma_start(ident[:, :], identity).then_inc(ident_loaded, 16)
            sp.dma_start(dense_rows[:, :, :], dense.rearrange("(p t) d -> p t d", t=TILES)).then_inc(dense_loaded, 16)
            sp.dma_start(mask[:, :, :], pair_mask).then_inc(mask_loaded, 16)
            load_ids(2)
            load_table(2)
            sp.dma_start(w1d[:, :, :], w1_dense.rearrange("(c p) n -> p c n", c=2)).then_inc(w1d_loaded, 16)
            sp.dma_start(w2s[:, :, :], w2.rearrange("(c p) n -> p c n", p=P)).then_inc(w2_loaded, 16)
            sp.dma_start(b2s[:, :], b2.unsqueeze(0)).then_inc(w2_loaded, 16)
            sp.dma_start(w3s[:, :], w3.rearrange("n o -> o n").to_broadcast([P, H2])).then_inc(w2_loaded, 16)
            for i in range(3, n_onehot):
                load_ids(i)
                load_table(i)
            sp.dma_start(w1_raw[:, :, :], w1_pairs).then_inc(w1_loaded, 16)
            load_ids(n_onehot)
            load_table(n_onehot)
            sp.wait_ge(y_ready, TILES)
            sp.dma_start(out.rearrange("(p t) n -> p (t n)", t=TILES), y[:, :]).then_inc(stored, 16)
            sp.wait_ge(stored, 16)

        @program.gpsimd
        def _(pool):
            pool.wait_ge(index_loaded, 16)
            for t in range(TILES):
                for g in range(len(GROUPS)):
                    if t >= 2:
                        pool.wait_ge(*written(("rows", t - 2, g)))
                    for k in group(t, g):
                        f = GATHERED[k]
                        pool.indirect_dma_start(
                            rows[:, t % 2, k, :], None, tables[f],
                            bass.IndirectOffsetOnAxis(ap=index[:, t, f:f + 1], axis=0),
                        ).then_inc(gathered[t][g], 16)
            pool.wait_ge(ps1_ready, LAST - 1)
            for n, (first, end) in enumerate(PARTS_POOL):
                pool.wait_ge(pairs_done, PAIR_COPIES * (4 * LAST + end // BATCH))
                whole = Z[:, :, LAST % 2, first:end]
                high = Zp[0][:, LAST % 2, :, first:end]
                nc.gpsimd.tensor_copy(high, whole).then_inc(Zhi_pool, 1)
                pool.wait_ge(Zhi_pool, n + 1)
                nc.gpsimd.tensor_tensor(Zp[1][:, LAST % 2, :, first:end], whole, high.bitcast(fp32),
                                        ALU.subtract).then_inc(Zlo_pool, 1)

        @program.scalar
        def _(act):
            def copy(dst, src):
                return nc.scalar.activation(dst, src, ACT.Copy)

            for step, *a in order():
                if step == "split":
                    i, = a
                    r = rows_per_part[i]
                    act.wait_ge(table_loaded[i % 2], 16 * (i // 2 + 1))
                    if i >= 2:
                        act.wait_ge(*written(("onehot", i - 2)))
                    copy(table_hi[i % 2][0:PART, 0:r, :], table[i % 2][0:PART, 0:r, :]).then_inc(hi_ready, 1)
                elif step == "make" and a[1] == 1:
                    i = a[0]
                    act.wait_ge(row_id_loaded, 16)
                    act.wait_ge(ids_loaded[i % 3], 16 * (i // 3 + 1))
                    for n, (_, c) in enumerate(act_blocks):
                        if act_blocks[n][0] != i:
                            continue
                        if n:
                            act.wait_ge(onehot_ready_act, n)
                        nc.scalar.activation(as_ids(block(distance, i), i), ids_of(i), ACT.Abs,
                                             bias=row_id[0:PART, 2 + int(rows_per_part[i] == max_rows), c:c + 1],
                                             ).then_inc(distance_ready, 1)
                        act.wait_ge(distance_ready, n + 1)
                        if n >= RING_ACT:
                            act.wait_ge(onehot_used, blocks.index(act_blocks[n - RING_ACT]) + 1)
                        nc.scalar.activation(block(onehot_act[n % RING_ACT], i), block(distance, i), ACT.Relu,
                                             bias=1.0, scale=-1.0).then_inc(onehot_ready_act, 1)
                elif step == "out" and a[0] == "hidden":
                    bank = tuple(a)
                    t, first, end = PIECES[a[1]]
                    act.wait_ge(*written(bank))
                    if t >= 1:
                        act.wait_ge(ps2_ready, t)
                    src = featT[:, banks.index(bank) % 2, 0:end - first].rearrange("n (c p) -> n c p", p=P)
                    copy(h1T[:, first // P:end // P, :], src).then_inc(featT_act, 1)
                elif step == "out":
                    act.wait_ge(*written(tuple(a)))
                    dst, src = bank_to_XT(tuple(a))
                    if a[0] == "dense":
                        copy(denseT[0][:, :, :], src).then_inc(dense_hi, 1)
                    for repeat in repeats_of(tuple(a)):
                        copy(*repeat)
                    copy(dst, src).then_inc(featT_act, 1)
                elif step == "weights":
                    piece, = a
                    act.wait_ge(*weights[piece][0])
                    _, high, _, raw = weights[piece]
                    copy(high, raw).then_inc(weights_hi, 1)
                elif step == "pairs":
                    batch, = a
                    t = BATCHES[batch][0]
                    if t >= 2:
                        act.wait_ge(Zlo_ready, 2 * (t - 1))
                    act.wait_ge(gram_ready, batch + 1)
                    for i in range(4):
                        for j in range(4):
                            dst, src = pair_block(batch, i, j, 4 + j)
                            copy(dst, src).then_inc(base_copied, 1)
                elif step == "relu":
                    piece, = a
                    t, first, end = PIECES[piece]
                    act.wait_ge(ps1_ready, piece + 1)
                    if t >= 2:
                        act.wait_ge(*written(("hidden", t - 2)))
                    nc.scalar.activation(h1[:, t % 2, first:end], ps1[piece], ACT.Relu).then_inc(h1_ready, 1)

        @program.vector
        def _(dve):
            def low(dst, whole, high):
                return nc.vector.tensor_tensor(dst, whole, high.bitcast(fp32), ALU.subtract)

            nc.vector.memset(ones[:, :], 1.0).then_inc(ones_ready, 1)
            nc.vector.memset(Z[:, :, :, :], 1.0).then_inc(bias_row, 1)
            dve.wait_ge(row_id_loaded, 16)
            for step, *a in order():
                if step == "split":
                    i, = a
                    r = rows_per_part[i]
                    dve.wait_ge(hi_ready, i + 1)
                    if i >= 2:
                        dve.wait_ge(*written(("onehot", i - 2)))
                    low(table_lo[i % 2][0:PART, 0:r, :], table[i % 2][0:PART, 0:r, :],
                        table_hi[i % 2][0:PART, 0:r, :]).then_inc(lo_ready, 1)
                elif step == "make":
                    i, rest = a
                    r = rows_per_part[i]
                    dve.wait_ge(ids_loaded[i % 3], 16 * (i // 3 + 1))
                    for n, (_, c) in enumerate(dve_blocks):
                        if dve_blocks[n][0] != i or (c >= made_first(i)) != rest:
                            continue
                        if n >= RING:
                            dve.wait_ge(onehot_used, blocks.index(dve_blocks[n - RING]) + 1)
                        nc.vector.tensor_scalar(as_ids(block(onehot_dve[n % RING], i), i), ids_of(i),
                                                row_id[0:PART, int(r == max_rows), c:c + 1], None,
                                                ALU.is_equal).then_inc(onehot_ready, 1)
                elif step == "out" and a[0] == "dense":
                    dve.wait_ge(dense_hi, 1)
                    dve.wait_ge(featT_act, 1)
                    low(denseT[1][:, :, :], featT[:, 0, :].rearrange("d (t p) -> d t p", t=TILES),
                        denseT[0][:, :, :]).then_inc(dense_lo, 1)
                elif step == "weights":
                    piece, = a
                    if piece == 0:
                        dve.wait_ge(w1d_loaded, 16)
                        nc.vector.tensor_tensor(w1d[:, 0, :], w1d[:, 0, :], w1d[:, 1, :],
                                                ALU.add).then_inc(w1_summed, 1)
                    dve.wait_ge(weights_hi, piece + 1)
                    _, high, lo, raw = weights[piece]
                    low(lo, raw, high).then_inc(weights_lo, 1)
                elif step == "pairs":
                    batch, = a
                    if batch == 0:
                        dve.wait_ge(mask_loaded, 16)

                    def choose(i, j, first, m):
                        dst, src = pair_block(batch, i, j, first)
                        m = m.unsqueeze(1).to_broadcast([rows_of(j), BATCH // 4, CHUNKS])
                        nc.vector.copy_predicated(dst, m, src).then_inc(pairs_done, 1)

                    for i in range(4):
                        dve.wait_ge(base_copied, 16 * batch + 4 * (i + 1))
                        for j in range(4):
                            choose(i, j, j, mask[32 * j:32 * j + rows_of(j), 0, :])
                        dve.wait_ge(pairs_done, PAIR_COPIES * batch + 5 * i + 1)
                        choose(i, 0, 8, mask[0:32, 1, :])
                elif step == "parts":
                    t, = a
                    if t == 0:
                        dve.wait_ge(bias_row, 1)
                    dve.wait_ge(pairs_done, pairs_of(t))
                    if t >= 2:
                        dve.wait_ge(ps1_ready, t - 1)
                    pieces = [(slice(0, 2), slice(0, P)), (slice(2, CHUNKS), slice(0, P))]
                    if t == LAST:
                        pieces = [(slice(0, CHUNKS), slice(P - BATCH, P))]
                    for n, (c, samples) in enumerate(pieces):
                        whole = Z[:, c, t % 2, samples]
                        high = Zp[0][:, t % 2, c, samples]
                        nc.vector.tensor_copy(high, whole).then_inc(Zhi_ready, 1)
                        dve.wait_ge(Zhi_ready, 2 * t + n + 1)
                        low(Zp[1][:, t % 2, c, samples], whole, high).then_inc(Zlo_ready, 1)
                elif step == "two":
                    t, = a
                    dve.wait_ge(ps2_ready, t + 1)
                    if t >= 1:
                        dve.wait_ge(y_ready, t)
                    nc.vector.scalar_tensor_tensor(h2w[:, :], ps2, 0.0, w3s[:, :], ALU.max,
                                                   ALU.mult).then_inc(h2_ready, 1)
                    dve.wait_ge(h2_ready, t + 1)
                    nc.vector.reduce_sum(y[:, t:t + 1], h2w[:, :], mybir.AxisListType.X).then_inc(y_ready, 1)

        @program.tensor
        def _(pe):
            def bank_free(bank):
                n = banks.index(bank)
                if n >= 2:
                    pe.wait_ge(*copied_out(banks[n - 2]))
                if n == 2:
                    pe.wait_ge(dense_lo, 1)

            def product(dst, x, w, first, last):
                for n, (i, j) in enumerate(((0, 0), (0, 1), (1, 0))):
                    mm = nc.tensor.matmul(dst, x[i], w[j], start=first and n == 0, stop=last and n == 2)
                return mm

            pe.wait_ge(ones_ready, 1)
            for _ in range(WARM_UP):
                nc.tensor.matmul(ps2[:, 0:P], ones[:, :], ones[:, :], start=True, stop=True)
            for step, *a in order():
                if step == "onehot":
                    i, = a
                    if i == n_onehot:
                        bank_free(("onehot", i))
                    elif i >= 4:
                        pe.wait_ge(*copied_out(("onehot", i - 4)))
                    pe.wait_ge(hi_ready, i + 1)
                    r = rows_per_part[i]
                    ahead = made_first(i)
                    products = [(c, part) for part in (table_hi, table_lo) for c in range(ahead)]
                    products += [(c, part) for c in range(ahead, r) for part in (table_hi, table_lo)]
                    bank = gram[:, i % 4, :]
                    if i == n_onehot:
                        bank = featT[:, banks.index(("onehot", i)) % 2, 0:(TILES - PARTLY_FROM) * P]
                    for c, part in products:
                        if by_act(r, c):
                            m = act_blocks.index((i, c))
                            pe.wait_ge(onehot_ready_act, m + 1)
                            x = onehot_act[m % RING_ACT]
                        else:
                            m = dve_blocks.index((i, c))
                            pe.wait_ge(onehot_ready, m + 1)
                            x = onehot_dve[m % RING]
                        if part is table_lo:
                            pe.wait_ge(lo_ready, i + 1)
                        mm = nc.tensor.matmul(bank, part[i % 2][0:PART, c, :], block(x, i),
                                              start=(c == 0 and part is table_hi),
                                              stop=(c == r - 1 and part is table_lo))
                        if part is table_lo:
                            mm.then_inc(onehot_used if (i, c) != (n_onehot, r - 1) else featT_ready, 1)
                elif step == "dense":
                    pe.wait_ge(ident_loaded, 16)
                    pe.wait_ge(dense_loaded, 16)
                    for t in range(TILES):
                        last = nc.tensor.transpose(featT[:, 0, t * P:(t + 1) * P], dense_rows[:, t, :], ident[:, :])
                    last.then_inc(featT_ready, 1)
                elif step == "rows":
                    t, g = a
                    n = banks.index(("rows", t, g))
                    bank_free(("rows", t, g))
                    pe.wait_ge(gathered[t][g], 16 * len(group(t, g)))
                    for s, k in enumerate(group(t, g)):
                        last = nc.tensor.transpose(featT[:, n % 2, s * P:(s + 1) * P], rows[:, t % 2, k, :],
                                                   ident[:, :])
                    last.then_inc(featT_ready, 1)
                elif step == "gram":
                    batch, = a
                    t, s0 = BATCHES[batch]
                    bank = gram_bank(batch)
                    for b in (("onehot", n_onehot if t >= PARTLY_FROM else n_onehot - 1),
                              ("rows", t, len(GROUPS) - 2), ("rows", t, len(GROUPS) - 1)):
                        pe.wait_ge(*copied_out(b))
                    if bank == 4:
                        n = banks.index(("hidden", LAST))
                        pe.wait_ge(*copied_out(banks[n - 2]))
                        pe.wait_ge(*copied_out(banks[n - 1]))
                    elif batch == len(BATCHES) - 1:
                        pe.wait_ge(pairs_done, PAIR_COPIES * (batch - 2))
                    elif batch >= 2:
                        pe.wait_ge(pairs_done, PAIR_COPIES * (batch - 1))
                    for q in range(BATCH // 4):
                        s = s0 + 4 * q
                        last = nc.tensor.matmul(psum[:, bank + q // 4, q % 4 * P:q % 4 * P + 4 * COLS],
                                                XT[:, t, s:s + 4, :], XT[:, t, s:s + 4, 0:COLS],
                                                start=True, stop=True)
                    last.then_inc(gram_ready, 1)
                elif step == "one":
                    piece, = a
                    t, first, end = PIECES[piece]
                    cols = slice(first, end)
                    if t == 0:
                        pe.wait_ge(weights_lo, len(weights))
                        pe.wait_ge(dense_lo, 1)
                    elif t < LAST:
                        pe.wait_ge(h1_ready, t)
                    else:
                        pe.wait_ge(pairs_done, PAIR_COPIES * (len(BATCHES) - 2))
                    product(ps1[piece], [x[:, t, :] for x in denseT], [w[:, cols] for w in w1s], True, False)
                    for c in range(CHUNKS):
                        if t < LAST:
                            pe.wait_ge(Zlo_ready, 2 * t + c // 2 + 1)
                        elif c == 0:
                            pe.wait_ge(Zlo_ready, 2 * LAST + 1)
                            pe.wait_ge(Zlo_pool, len(PARTS_POOL))
                        last = product(ps1[piece], [x[:, t % 2, c, :] for x in Zp],
                                       [w[:, c, cols] for w in w1p], False, c == CHUNKS - 1)
                    last.then_inc(ps1_ready, 1)
                elif step == "hidden":
                    piece, = a
                    t, first, end = PIECES[piece]
                    n = banks.index(("hidden", piece))
                    bank_free(("hidden", piece))
                    pe.wait_ge(h1_ready, piece + 1)
                    for c in range(first, end, P):
                        last = nc.tensor.transpose(featT[:, n % 2, c - first:c - first + P], h1[:, t % 2, c:c + P],
                                                   ident[:, :])
                    last.then_inc(featT_ready, 1)
                elif step == "bias":
                    t, = a
                    if t == 0:
                        pe.wait_ge(ones_ready, 1)
                        pe.wait_ge(w2_loaded, 16 * 3)
                    else:
                        pe.wait_ge(h2_ready, t)
                    nc.tensor.matmul(ps2, ones[0:1, :], b2s[:, :], start=True, stop=False)
                elif step == "two":
                    t, = a
                    for c in range(H1 // P):
                        for piece, (tile, first, _) in enumerate(PIECES):
                            if tile == t and first == c * P:
                                pe.wait_ge(*copied_out(("hidden", piece)))
                        last = nc.tensor.matmul(ps2, h1T[:, c, :], w2s[:, c, :], start=False,
                                                stop=c == H1 // P - 1)
                    last.then_inc(ps2_ready, 1)


def slot_repeated(s):
    return next((slot for slot, repeats in REPEATS.items() if s in repeats), s)


def pair_places():
    places = {}
    for k in range(PAIR_COLS):
        m, j = divmod(k, 4)
        for s in range(rows_of(j)):
            for x in (j, j + 4, 8)[:3 if j == 0 else 2]:
                if x + 9 * m != slot_repeated(s):
                    places.setdefault(frozenset((slot_repeated(s), x + 9 * m)), []).append(((s, k), x + 9 * m))
    holds = {}

    def place(pair, seen):
        for at, column in places[pair]:
            if at not in seen:
                seen.add(at)
                if at not in holds or place(holds[at][0], seen):
                    holds[at] = pair, column
                    return True
        return False

    for a in range(F):
        for b in range(a + 1, F):
            assert place(frozenset((a, b)), set())
    return {at: column for at, (_, column) in holds.items()}


def kernel(**inputs):
    import numpy as np
    import concourse.bacc as bacc
    from concourse.bass_utils import run_bass_kernel_spmd

    w1 = np.asarray(inputs["W_top1"])
    w1_pairs = np.zeros((P, CHUNKS, H1), w1.dtype)
    pair_mask = np.zeros((P, 2, CHUNKS), np.int32)
    w1_pairs[BIAS_ROW, 0] = inputs["b_top1"]
    for (s, k), partner in pair_places().items():
        c, j = divmod(k, 4)
        a, b = sorted((FEATURE_OF_SLOT[slot_repeated(s)], FEATURE_OF_SLOT[partner]))
        w1_pairs[32 * j + s, c] = w1[D + a * F - a * (a + 1) // 2 + b - a - 1]
        pair_mask[32 * j + s, 0, c] = partner % 9 == j
        pair_mask[32 * j + s, 1, c] = partner % 9 == 8
    w1_dense = np.concatenate([w1[0:D], w1[-D:]])
    ids = np.asarray(inputs["ids"])
    sizes = [inputs[f"tbl_{f}"].shape[0] // PART for f in ONEHOT]
    row_ids = np.zeros((P, 4, max(sizes)), np.float32)
    for w, r in enumerate((min(sizes), max(sizes))):
        row_ids[:, w, 0:r] = np.arange(P)[:, None] * r + np.arange(r)[None, :]
        row_ids[:, 2 + w, 0:r] = -row_ids[:, w, 0:r]

    nc = bacc.Bacc("TRN2", target_bir_lowering=False, num_devices=1)
    arrays = {}

    def given(name, a):
        arrays[name] = np.ascontiguousarray(a)
        return nc.dram_tensor(name, arrays[name].shape, mybir.dt.from_np(arrays[name].dtype),
                              kind="ExternalInput").ap()

    out = nc.dram_tensor("out_0", (B, 1), mybir.dt.float32, kind="ExternalOutput").ap()
    tower(
        nc,
        given("dense", inputs["r_dense_features"]),
        given("ids", ids),
        given("ids_by_table", ids.T[ONEHOT + [PARTLY]]),
        [given(f"tbl_{f}", inputs[f"tbl_{f}"]) for f in range(N_TABLES)],
        given("w1_pairs", w1_pairs),
        given("w1_dense", w1_dense),
        given("w2", inputs["W_top2"]),
        given("b2", inputs["b_top2"]),
        given("w3", inputs["W_top3"]),
        given("identity", np.eye(P, dtype=np.float32)),
        given("row_ids", row_ids),
        given("pair_mask", pair_mask),
        out,
    )
    result = run_bass_kernel_spmd(nc, [arrays], core_ids=[0])
    return result.results[0]["out_0"]
```
